# Optimizing a Trainium2 kernel written in Bass

```python
import numpy as np
import jax
import jax.numpy as jnp

def _softmax(x, axis=-1):
    return jax.nn.softmax(x, axis=axis)

def _gelu(x):
    return jax.nn.gelu(x, approximate=True)

def _silu(x):
    return jax.nn.silu(x)

def _sigmoid(x):
    return jax.nn.sigmoid(x)

def _layernorm(x, axis=-1, eps=1e-05):
    m = jnp.mean(x, axis=axis, keepdims=True)
    v = jnp.var(x, axis=axis, keepdims=True)
    return (x - m) / jnp.sqrt(v + eps)

def _scatter_add(tgt, idx, src, axis=0):
    return tgt.at[idx].add(src)

def _segment_sum(src, seg, n):
    return jax.ops.segment_sum(src, seg, n)
kernel_name = 'mk_sandwich_d1_jaxref_r4_d11921'

def setup_inputs(seed: int=0):
    np.random.seed(seed)
    _w = jnp.asarray

    def _L0_attn_setup():
        import jax, jax.numpy as jnp
        import numpy as np
        B, N, D, H = (2, 512, 256, 16)
        HD = D // H
        SCALING = (D / H) ** 0.5
        EPS = 1e-05
        key = jax.random.key(seed)
        k1, k2, k3 = jax.random.split(key, 3)
        return {'z': jax.random.normal(k1, (B, N, D), dtype=jnp.float32), 'ln_scale': jnp.ones((D,), dtype=jnp.float32), 'ln_bias': jnp.zeros((D,), dtype=jnp.float32), 'w_qkv': jax.random.normal(k2, (D, 3 * D), dtype=jnp.float32) * D ** (-0.5), 'w_proj': jax.random.normal(k3, (D, D), dtype=jnp.float32) * D ** (-0.5), 'b_proj': jnp.zeros((D,), dtype=jnp.float32)}
    _L0_attn_in = _L0_attn_setup()

    def _L0_ffn_setup():
        import jax, jax.numpy as jnp
        import numpy as np
        EPS = 1e-05

        def _ln(x, g, b):
            mu = jnp.mean(x, axis=-1, keepdims=True)
            var = jnp.mean(jnp.square(x - mu), axis=-1, keepdims=True)
            return (x - mu) * jax.lax.rsqrt(var + EPS) * g + b

        def _forward(x, index_b, index_t, sw1, sb1, sw2, sb2, sw3, sb3, s_ln_g, s_ln_b, sg_w, sg_b, eg_w, eg_b, exp_bias, ew1, eb1, ew2, eb2, ew3, eb3, sel_ln_g, sel_ln_b):
            x1 = jnp.einsum('btd,hd->bth', x, sw1) + sb1
            x2 = jnp.einsum('btd,hd->bth', x, sw2) + sb2
            sh = _ln(jax.nn.silu(x1) * x2, s_ln_g, s_ln_b)
            shared_out = jnp.einsum('bth,dh->btd', sh, sw3) + sb3
            x_moe = x[index_b, index_t]
            shared_scores = jax.nn.sigmoid(x_moe @ sg_w.T + sg_b)
            expert_scores = jax.nn.sigmoid(x_moe @ eg_w.T + eg_b)
            top1_idx = jnp.argmax(expert_scores + exp_bias, axis=-1)
            top1_score = jnp.take_along_axis(expert_scores, top1_idx[:, None], axis=-1)
            weights = jax.nn.softmax(jnp.concatenate([shared_scores, top1_score], axis=-1), axis=-1)
            shared_w, expert_w = (weights[:, 0], weights[:, 1])
            shared_moe_out = shared_out[index_b, index_t] * shared_w[:, None]
            h1 = jnp.einsum('md,ehd->meh', x_moe, ew1) + eb1
            h2 = jnp.einsum('md,ehd->meh', x_moe, ew2) + eb2
            z = _ln(jax.nn.silu(h1) * h2, sel_ln_g, sel_ln_b)
            out_all = jnp.einsum('meh,edh->med', z, ew3) + eb3
            expert_out = jnp.take_along_axis(out_all, top1_idx[:, None, None], axis=1)[:, 0]
            expert_moe_out = expert_out * expert_w[:, None]
            final_out = shared_out.at[index_b, index_t].set(shared_moe_out + expert_moe_out)
            return final_out
        B, T, D, E, H, M = (2, 512, 256, 8, 128, 512)
        key = jax.random.key(seed)
        ks = jax.random.split(key, 24)
        s = 0.02
        inp = {}
        inp['x'] = jax.random.normal(ks[0], (B, T, D), jnp.float32)
        flat = jnp.arange(M, dtype=jnp.int32) * 2
        inp['index_b'] = flat // T
        inp['index_t'] = flat % T
        inp['sw1'] = jax.random.normal(ks[1], (H, D), jnp.float32) * s
        inp['sb1'] = jnp.zeros((H,), jnp.float32)
        inp['sw2'] = jax.random.normal(ks[2], (H, D), jnp.float32) * s
        inp['sb2'] = jnp.zeros((H,), jnp.float32)
        inp['sw3'] = jax.random.normal(ks[3], (D, H), jnp.float32) * s
        inp['sb3'] = jnp.zeros((D,), jnp.float32)
        inp['s_ln_g'] = jnp.ones((H,), jnp.float32)
        inp['s_ln_b'] = jnp.zeros((H,), jnp.float32)
        inp['sg_w'] = jax.random.normal(ks[4], (1, D), jnp.float32) * s
        inp['sg_b'] = jnp.zeros((1,), jnp.float32)
        inp['eg_w'] = jax.random.normal(ks[5], (E, D), jnp.float32) * s
        inp['eg_b'] = jnp.zeros((E,), jnp.float32)
        inp['exp_bias'] = jnp.zeros((E,), jnp.float32)
        inp['ew1'] = jax.random.normal(ks[6], (E, H, D), jnp.float32) * s
        inp['eb1'] = jnp.zeros((E, H), jnp.float32)
        inp['ew2'] = jax.random.normal(ks[7], (E, H, D), jnp.float32) * s
        inp['eb2'] = jnp.zeros((E, H), jnp.float32)
        inp['ew3'] = jax.random.normal(ks[8], (E, D, H), jnp.float32) * s
        inp['eb3'] = jnp.zeros((E, D), jnp.float32)
        inp['sel_ln_g'] = jnp.ones((H,), jnp.float32)
        inp['sel_ln_b'] = jnp.zeros((H,), jnp.float32)
        return inp
    _L0_ffn_in = _L0_ffn_setup()
    _d = {'L0_attn_z': _L0_attn_in['z'], 'L0_attn_ln_scale': _L0_attn_in['ln_scale'], 'L0_attn_ln_bias': _L0_attn_in['ln_bias'], 'L0_attn_w_qkv': _L0_attn_in['w_qkv'], 'L0_attn_w_proj': _L0_attn_in['w_proj'], 'L0_attn_b_proj': _L0_attn_in['b_proj'], 'L0_ffn_index_b': _L0_ffn_in['index_b'], 'L0_ffn_index_t': _L0_ffn_in['index_t'], 'L0_ffn_sw1': _L0_ffn_in['sw1'], 'L0_ffn_sb1': _L0_ffn_in['sb1'], 'L0_ffn_sw2': _L0_ffn_in['sw2'], 'L0_ffn_sb2': _L0_ffn_in['sb2'], 'L0_ffn_sw3': _L0_ffn_in['sw3'], 'L0_ffn_sb3': _L0_ffn_in['sb3'], 'L0_ffn_s_ln_g': _L0_ffn_in['s_ln_g'], 'L0_ffn_s_ln_b': _L0_ffn_in['s_ln_b'], 'L0_ffn_sg_w': _L0_ffn_in['sg_w'], 'L0_ffn_sg_b': _L0_ffn_in['sg_b'], 'L0_ffn_eg_w': _L0_ffn_in['eg_w'], 'L0_ffn_eg_b': _L0_ffn_in['eg_b'], 'L0_ffn_exp_bias': _L0_ffn_in['exp_bias'], 'L0_ffn_ew1': _L0_ffn_in['ew1'], 'L0_ffn_eb1': _L0_ffn_in['eb1'], 'L0_ffn_ew2': _L0_ffn_in['ew2'], 'L0_ffn_eb2': _L0_ffn_in['eb2'], 'L0_ffn_ew3': _L0_ffn_in['ew3'], 'L0_ffn_eb3': _L0_ffn_in['eb3'], 'L0_ffn_sel_ln_g': _L0_ffn_in['sel_ln_g'], 'L0_ffn_sel_ln_b': _L0_ffn_in['sel_ln_b']}
    _x0 = _d['L0_attn_z']
    _d['L0_attn_z'] = jax.random.normal(jax.random.fold_in(jax.random.key(seed), 1), (4, 1024, 256), dtype=_x0.dtype)
    del _x0
    return _d

def reference(L0_attn_z, L0_attn_ln_scale, L0_attn_ln_bias, L0_attn_w_qkv, L0_attn_w_proj, L0_attn_b_proj, L0_ffn_index_b, L0_ffn_index_t, L0_ffn_sw1, L0_ffn_sb1, L0_ffn_sw2, L0_ffn_sb2, L0_ffn_sw3, L0_ffn_sb3, L0_ffn_s_ln_g, L0_ffn_s_ln_b, L0_ffn_sg_w, L0_ffn_sg_b, L0_ffn_eg_w, L0_ffn_eg_b, L0_ffn_exp_bias, L0_ffn_ew1, L0_ffn_eb1, L0_ffn_ew2, L0_ffn_eb2, L0_ffn_ew3, L0_ffn_eb3, L0_ffn_sel_ln_g, L0_ffn_sel_ln_b):

    def _L0_attn_ref(z, ln_scale, ln_bias, w_qkv, w_proj, b_proj):
        import jax, jax.numpy as jnp
        import numpy as np
        B, N, D, H = (2, 512, 256, 16)
        HD = D // H
        SCALING = (D / H) ** 0.5
        EPS = 1e-05
        b, n, d = z.shape
        mu = jnp.mean(z, axis=-1, keepdims=True)
        var = jnp.mean(jnp.square(z - mu), axis=-1, keepdims=True)
        zn = (z - mu) / jnp.sqrt(var + EPS) * ln_scale + ln_bias
        qkv = zn @ w_qkv
        qkv5 = qkv.reshape(b, n, H, HD, 3)
        q = jnp.transpose(qkv5[..., 0], (0, 2, 1, 3))
        k = jnp.transpose(qkv5[..., 1], (0, 2, 1, 3))
        v = jnp.transpose(qkv5[..., 2], (0, 2, 1, 3))
        scores = jnp.einsum('bhqd,bhkd->bhqk', q, k) / SCALING
        att = jax.nn.softmax(scores, axis=-1)
        out = jnp.einsum('bhal,bhlv->bhav', att, v)
        out = jnp.transpose(out, (0, 2, 1, 3)).reshape(b, n, d)
        out = out @ w_proj + b_proj
        return z + out

    def _L0_ffn_ref(x, index_b, index_t, sw1, sb1, sw2, sb2, sw3, sb3, s_ln_g, s_ln_b, sg_w, sg_b, eg_w, eg_b, exp_bias, ew1, eb1, ew2, eb2, ew3, eb3, sel_ln_g, sel_ln_b):
        import jax, jax.numpy as jnp
        import numpy as np
        EPS = 1e-05

        def _ln(x, g, b):
            mu = jnp.mean(x, axis=-1, keepdims=True)
            var = jnp.mean(jnp.square(x - mu), axis=-1, keepdims=True)
            return (x - mu) * jax.lax.rsqrt(var + EPS) * g + b

        def _forward(x, index_b, index_t, sw1, sb1, sw2, sb2, sw3, sb3, s_ln_g, s_ln_b, sg_w, sg_b, eg_w, eg_b, exp_bias, ew1, eb1, ew2, eb2, ew3, eb3, sel_ln_g, sel_ln_b):
            x1 = jnp.einsum('btd,hd->bth', x, sw1) + sb1
            x2 = jnp.einsum('btd,hd->bth', x, sw2) + sb2
            sh = _ln(jax.nn.silu(x1) * x2, s_ln_g, s_ln_b)
            shared_out = jnp.einsum('bth,dh->btd', sh, sw3) + sb3
            x_moe = x[index_b, index_t]
            shared_scores = jax.nn.sigmoid(x_moe @ sg_w.T + sg_b)
            expert_scores = jax.nn.sigmoid(x_moe @ eg_w.T + eg_b)
            top1_idx = jnp.argmax(expert_scores + exp_bias, axis=-1)
            top1_score = jnp.take_along_axis(expert_scores, top1_idx[:, None], axis=-1)
            weights = jax.nn.softmax(jnp.concatenate([shared_scores, top1_score], axis=-1), axis=-1)
            shared_w, expert_w = (weights[:, 0], weights[:, 1])
            shared_moe_out = shared_out[index_b, index_t] * shared_w[:, None]
            h1 = jnp.einsum('md,ehd->meh', x_moe, ew1) + eb1
            h2 = jnp.einsum('md,ehd->meh', x_moe, ew2) + eb2
            z = _ln(jax.nn.silu(h1) * h2, sel_ln_g, sel_ln_b)
            out_all = jnp.einsum('meh,edh->med', z, ew3) + eb3
            expert_out = jnp.take_along_axis(out_all, top1_idx[:, None, None], axis=1)[:, 0]
            expert_moe_out = expert_out * expert_w[:, None]
            final_out = shared_out.at[index_b, index_t].set(shared_moe_out + expert_moe_out)
            return final_out
        return _forward(x, index_b, index_t, sw1, sb1, sw2, sb2, sw3, sb3, s_ln_g, s_ln_b, sg_w, sg_b, eg_w, eg_b, exp_bias, ew1, eb1, ew2, eb2, ew3, eb3, sel_ln_g, sel_ln_b)
    x = L0_attn_z
    x = x + _layernorm(_L0_attn_ref(_layernorm(x, axis=-1), L0_attn_ln_scale, L0_attn_ln_bias, L0_attn_w_qkv, L0_attn_w_proj, L0_attn_b_proj), axis=-1)
    x = x + _layernorm(_L0_ffn_ref(_layernorm(x, axis=-1), L0_ffn_index_b, L0_ffn_index_t, L0_ffn_sw1, L0_ffn_sb1, L0_ffn_sw2, L0_ffn_sb2, L0_ffn_sw3, L0_ffn_sb3, L0_ffn_s_ln_g, L0_ffn_s_ln_b, L0_ffn_sg_w, L0_ffn_sg_b, L0_ffn_eg_w, L0_ffn_eg_b, L0_ffn_exp_bias, L0_ffn_ew1, L0_ffn_eb1, L0_ffn_ew2, L0_ffn_eb2, L0_ffn_ew3, L0_ffn_eb3, L0_ffn_sel_ln_g, L0_ffn_sel_ln_b), axis=-1)
    return x

_drawn_inputs = setup_inputs


def setup_inputs(seed=0):
    import zlib

    import numpy as np

    out = dict(_drawn_inputs(seed))
    spreads = {'L0_attn_ln_scale': (1.0, 0.6),
     'L0_attn_ln_bias': (0.0, 0.1),
     'L0_attn_b_proj': (0.0, 0.1),
     'L0_ffn_sb1': (0.0, 0.1),
     'L0_ffn_sb2': (0.0, 0.1),
     'L0_ffn_sb3': (0.0, 0.1),
     'L0_ffn_s_ln_g': (1.0, 0.2),
     'L0_ffn_s_ln_b': (0.0, 0.1),
     'L0_ffn_eg_b': (0.0, 0.1),
     'L0_ffn_exp_bias': (0.0, 0.1),
     'L0_ffn_eb1': (0.0, 0.1),
     'L0_ffn_eb2': (0.0, 0.1),
     'L0_ffn_eb3': (0.0, 0.1),
     'L0_ffn_sel_ln_g': (1.0, 0.6),
     'L0_ffn_sel_ln_b': (0.0, 0.759)}
    factors = {'L0_ffn_sg_w': 8.0}
    for name, (base, spread) in spreads.items():
        noise = np.random.default_rng([zlib.crc32(name.encode()), seed]).standard_normal(out[name].shape)
        drawn = base * np.exp(spread * noise) if base else spread * noise
        out[name] = jnp.asarray(drawn.astype(out[name].dtype))
    for name, factor in factors.items():
        out[name] = (out[name] * factor).astype(out[name].dtype)
    return out
```

```python
from contextlib import ExitStack

import concourse.bass as bass
from concourse import mybir

P = 128
B, N, D = 4, 1024, 256
H, HD = 16, 16
E, F = 8, 128
M = 512
NT = N // P
KD = D // P
EPS = 1e-5
GH = 4
G = H // GH
HALF = 512
NH = N // HALF
HU = G * NH
QT = HALF // P
NPART = 6
KR = NPART * HD
KM = KR + 2
VW = 32
STEPS = HU * NT
LEAD = 12
SLOTS = STEPS + LEAD + 3
K_PARTS = [0, 1, 2, 0, 1, 0]
Q_PARTS = [0, 0, 0, 1, 1, 2]
MT = M // P


def attention_ring_order():
    order = []
    for slot in range(SLOTS):
        if slot < STEPS:
            order += [("max", slot, j) for j in range(4)]
        if slot % 8 == 1 and 0 <= slot // 8 - 1 < HU:
            order.append(("mt", slot // 8 - 1))
        e = slot - LEAD
        if e >= 0 and e % 8 == 2 and 0 <= e // 8 - 1 < HU:
            order.append(("ot", e // 8 - 1))
    return order


ATT = attention_ring_order()
R_V = 0
R_ATT = R_V + NT // 2
R_PROJ = R_ATT + len(ATT)
R_FFN = R_PROJ + NT // 2
R_BATCH = R_FFN + NT
S_ZT = 0
S_QK = S_ZT + KD
S_ATT = S_QK + 2 * KD
S_AT = S_ATT + 2 * STEPS
S_XT = S_AT + KD
S_UT = S_XT + KD
S_BATCH = S_UT + 1


def build(nc, x, ln_params, w_q, w_k, w_v, w_proj, b_proj, index_b, index_t, sw12, sb12, sw3, sb3,
          hidden_ln, gate_w, gate_b, exp_bias, ew12, ebias12, ew3, eb3, out):
    f32, bf16, i32, u32 = mybir.dt.float32, mybir.dt.bfloat16, mybir.dt.int32, mybir.dt.uint32
    ALU, ACT, AX = mybir.AluOpType, mybir.ActivationFunctionType, mybir.AxisListType

    x1_dram = nc.dram_tensor("x1_scratch", [B * N, D], f32, kind="Internal").ap()
    x_tiles = x.rearrange("b (t p) d -> b p t d", p=P)
    out_tiles = out.rearrange("b (t p) d -> b p t d", p=P)
    x1_tiles = x1_dram.rearrange("(b t p) d -> b p t d", p=P, t=NT)
    out_rows = out.rearrange("b n d -> (b n) d")

    with ExitStack() as ctx:
        def sb(name, shape, dt=f32):
            return ctx.enter_context(nc.sbuf_tensor(name, shape, dt))

        def sem(name):
            return ctx.enter_context(nc.semaphore(name))

        x_sb = sb("x_sb", [P, NT, D])
        zb = sb("zb", [P, NT, D])
        zn = sb("zn", [P, NT, D])
        zT = sb("zT", [P, KD, N])
        x1 = sb("x1", [P, NT, D])
        hid = sb("hid", [P, NT, D])
        anat = sb("anat", [P, NT, D])
        act = anat[:, :, 0:F]
        qkf = sb("qkf", [P, 2, N])
        resid = sb("resid", [P, N])
        parts = sb("parts", [P, 2, 3, N], bf16)
        qp = sb("qp", [P, NH, H, HALF], bf16)
        kp = sb("kp", [P, H, N], bf16)
        vaug = sb("vaug", [P, NT, H, VW])
        prob = sb("prob", [P, 2, GH, HALF])
        oT = sb("oT", [P, 2, HALF])
        wq = sb("wq", [P, KD, D])
        wk = sb("wk", [P, KD, D])
        wv = sb("wv", [P, KD, D])
        wp = sb("wp", [P, KD, D])
        w12 = sb("w12", [P, KD, 2 * F])
        w3 = sb("w3", [P, D])
        wg = sb("wg", [P, KD, 1 + E])
        bproj = sb("bproj", [P, D])
        b12 = sb("b12", [P, 2 * F])
        b3 = sb("b3", [P, D])
        bgate = sb("bgate", [P, 1 + E])
        bexp = sb("bexp", [P, E])
        eb12 = sb("eb12", [E, 2 * F])
        ebo = sb("ebo", [E, D])
        lnp = sb("lnp", [P, 2, KD])
        hln = sb("hln", [P, 4])
        mhalf = sb("mhalf", [P, NT])
        ident = sb("ident", [P, P])
        pick = sb("pick", [E, E, P])
        iota = sb("iota", [P, E])
        iotai = sb("iotai", [P, E], i32)
        mx = sb("mx", [P, 2, GH * QT * 2])
        nm = sb("nm", [P, 2, GH * QT])
        mp = sb("mp", [GH * QT, 2, 2, P], bf16)
        rsum = sb("rsum", [P, QT * GH])
        st6 = sb("st6", [P, NT, 6])
        LN = ["z", "y", "x", "u", "f"]
        mv = {k: sb("mv_" + k, [P, NT, 2]) for k in LN}
        lv = {k: sb("lv_" + k, [P, NT]) for k in LN}
        rstd = {k: sb("rstd_" + k, [P, NT]) for k in LN}
        lv2, rstd2, rr, vn = (sb(n, [P, NT]) for n in ("lv2", "rstd2", "rr", "vn"))
        r12, shift = (sb(n, [P, NT]) for n in ("r12", "shift"))
        idx_in = sb("idx_in", [P, 2, MT], i32)
        idxf = sb("idxf", [P, 2, MT])
        idxn = sb("idxn", [P, 2, MT])
        idx = sb("idx", [P, MT], i32)
        gate = sb("gate", [P, MT, 1 + E])
        gexp = sb("gexp", [P, MT, 1 + E])
        gsel = sb("gsel", [P, MT, E])
        top8 = sb("top8", [P, MT, 8])
        topi = sb("topi", [P, MT, 8], u32)
        topf = sb("topf", [P, MT])
        onehot = sb("onehot", [P, MT, E])
        ohs = sb("ohs", [P, MT, E])
        sc2 = sb("sc2", [P, MT, 2])
        ex2 = sb("ex2", [P, MT, 2])
        sum2 = sb("sum2", [P, MT])
        wt2 = sb("wt2", [P, MT, 2])
        ohT = qkf[0:E, 0, 0:M]
        bc = prob[:, :, :, :].rearrange("p a g n -> p (a g) n")
        xm = qp[:, :, :, :].rearrange("p a h n -> p (a h n)").bitcast(f32)\
            .rearrange("p (k e m) -> p k e m", k=KD, e=E)
        kflat = kp[:, :, :].rearrange("p h n -> p (h n)").bitcast(f32)
        we12 = kflat[:, 0:KD * E * 2 * F].rearrange("p (k e f) -> p k e f", k=KD, e=E)
        we3 = kflat[:, KD * E * 2 * F:KD * E * 2 * F + E * D].rearrange("p (e d) -> p e d", e=E)
        zm = xm[:, 0, :, :]
        mout = resid[:, 0:D]

        sbuf2 = [ctx.enter_context(nc.psum_tensor(f"sc{i}", [P, 2 * HALF], f32)) for i in range(2)]
        ring = [ctx.enter_context(nc.psum_tensor(f"ring{i}", [P, HALF], f32)) for i in range(3)]
        obank = ctx.enter_context(nc.psum_tensor("obank", [P, HALF], f32))

        s_const = sem("constants_loaded")
        s_made = sem("constants_made")
        s_iota = sem("iota_made")
        s_vset = sem("value_operand_preset")
        s_xin = sem("x_loaded")
        s_full = sem("score_buffer_filled")
        s_free = sem("score_buffer_taken")
        r_full = sem("ring_filled")
        r_free = sem("ring_taken")
        s_stats = {k: sem("stats_" + k) for k in LN}
        s_mean = {k: sem("mean_" + k) for k in LN}
        s_log = {k: sem("variance_plus_eps_" + k) for k in LN}
        s_rstd = {k: sem("rstd_of_" + k) for k in LN}
        s_norm = {k: sem("normalized_" + k) for k in LN}
        s_small = sem("small_vector_steps")
        s_vn = sem("variance_of_z")
        s_log2 = sem("variance_of_z_plus_eps")
        s_rstd2 = sem("second_rstd_of_z")
        s_shift = sem("shift_of_z")
        s_zs = sem("z_scaled")
        s_zb = sem("z_with_bias")
        s_zT = sem("transposed")
        s_first = sem("first_part")
        s_resid = sem("residual_of_first_part")
        s_second = sem("second_part")
        s_third = sem("third_part")
        s_pack = [sem("parts_stacked_even"), sem("parts_stacked_odd")]
        s_hmax = sem("half_unit_maxima")
        s_nm = sem("negated_maxima")
        s_m1 = sem("maxima_first_part")
        s_mrow = [sem("maxima_rows_even"), sem("maxima_rows_odd")]
        s_exp = sem("exponentials_ready")
        s_av = sem("value_product_step")
        s_oT = sem("output_evacuated")
        s_rs = sem("reciprocal_sums")
        s_x1 = sem("x1_ready")
        s_he = sem("hidden_tanh")
        s_hc = sem("hidden_chain")
        s_res = sem("result_ready")
        s_x1st = sem("x1_stored")
        s_out = sem("out_stored")
        s_idx = sem("index_steps")
        s_idxin = sem("indices_loaded")
        s_we = sem("expert_weights_loaded")
        s_xg = sem("routed_rows_gathered")
        s_g = sem("gate_steps")
        s_ge = sem("gate_exponentials")
        s_bc = sem("one_hot_spread")
        s_xm = sem("masked_by_expert")
        s_mix = sem("mix_steps")
        s_held = sem("waits_held")
        s_scat = sem("routed_rows_stored")

        block = ctx.enter_context(nc.Block())

        const_loads = [
            (wk[:, :, :], w_k.rearrange("(k p) n -> p k n", p=P)),
            (wq[:, :, :], w_q.rearrange("(k p) n -> p k n", p=P)),
            (lnp[:, :, :], ln_params),
            (bproj[:, :], b_proj.partition_broadcast(P)),
            (wv[:, :, :], w_v.rearrange("(k p) n -> p k n", p=P)),
            (wp[:, :, :], w_proj.rearrange("(k p) n -> p k n", p=P)),
            (w12[:, :, :], sw12.rearrange("(k p) n -> p k n", p=P)),
            (w3[:, :], sw3),
            (wg[:, :, :], gate_w.rearrange("(k p) n -> p k n", p=P)),
            (b12[:, :], sb12.partition_broadcast(P)),
            (b3[:, :], sb3.partition_broadcast(P)),
            (bgate[:, :], gate_b.partition_broadcast(P)),
            (bexp[:, :], exp_bias.partition_broadcast(P)),
            (eb12[:, :], ebias12),
            (ebo[:, :], eb3),
            (hln[:, :], hidden_ln),
        ]
        C_ALL = 16 * len(const_loads)

        @block.sync
        def _(sp):
            sp.dma_start(idx_in[:, 0, :], index_b.rearrange("(p c) -> p c", p=P)).then_inc(s_idxin, 16)
            sp.dma_start(idx_in[:, 1, :], index_t.rearrange("(p c) -> p c", p=P)).then_inc(s_idxin, 16)
            for dst, src in const_loads:
                sp.dma_start(dst, src).then_inc(s_const, 16)
            with sp.Fori(0, B) as b:
                sp.dma_start(x_sb[:, :, :], x_tiles[b, :, :, :]).then_inc(s_xin, 16)
                for c in range(2 * KD):
                    sp.wait_ge(s_third, 2 * KD * b + c + 1)
                    mt = c % KD
                    for r in range(NPART):
                        rows = slice(r * HD, (r + 1) * HD)
                        if c < KD:
                            sp.dma_start(kp[rows, mt * 8:mt * 8 + 8, :], parts[:, c % 2, K_PARTS[r], :])\
                              .then_inc(s_pack[c % 2], 16)
                        else:
                            for h in range(NH):
                                sp.dma_start(qp[rows, h, mt * 8:mt * 8 + 8, :],
                                             parts[:, c % 2, Q_PARTS[r], h * HALF:(h + 1) * HALF])\
                                  .then_inc(s_pack[c % 2], 16)
                for u in range(HU):
                    g, qh = u // NH, u % NH
                    sp.wait_ge(r_free, R_BATCH * b + R_ATT + ATT.index(("mt", u)) + 1)
                    for j in range(2):
                        sp.dma_start(qp[KR + j:KR + j + 1, qh, g * GH:(g + 1) * GH, :],
                                     mp[:, u % 2, j, :]).then_inc(s_mrow[u % 2], 16)
                sp.wait_ge(s_x1, b + 1)
                sp.dma_start(x1_tiles[b, :, :, :], x1[:, :, :]).then_inc(s_x1st, 16)
                sp.wait_ge(s_res, b + 1)
                sp.dma_start(out_tiles[b, :, :, :], hid[:, :, :]).then_inc(s_out, 16)
                sp.wait_ge(s_x1st, 16 * (b + 1))
                sp.wait_ge(s_out, 16 * (b + 1))
                sp.sem_inc(s_held, 1)
            sp.wait_ge(s_av, STEPS * B)
            sp.dma_start(we12, ew12.rearrange("(k p) e f -> p k e f", p=P)).then_inc(s_we, 16)
            sp.dma_start(we3, ew3).then_inc(s_we, 16)
            sp.wait_ge(s_scat, 16 * MT)

        @block.gpsimd
        def _(pool):
            nc.gpsimd.memset(ident[:, :], 0.0)
            nc.gpsimd.memset(pick[:, :, :], 0.0)
            nc.gpsimd.memset(mhalf[:, :], -0.5)
            nc.gpsimd.iota(iotai[:, :], pattern=[[1, E]], base=0, channel_multiplier=0).then_inc(s_iota, 1)
            pool.wait_ge(s_iota, 1)
            nc.gpsimd.affine_select(out=ident[:, :], in_=ident[:, :], compare_op=ALU.not_equal, fill=1.0,
                                    base=0, pattern=[[-1, P]], channel_multiplier=1)
            nc.gpsimd.affine_select(out=pick[:, :, :], in_=pick[:, :, :], compare_op=ALU.not_equal, fill=1.0,
                                    base=0, pattern=[[-1, E], [0, P]], channel_multiplier=1)\
                .then_inc(s_made, 1)
            pool.wait_ge(s_made, 1)
            nc.gpsimd.memset(kp[KR:KM, :, :], 1.0).then_inc(s_made, 1)
            pool.wait_ge(s_const, C_ALL)
            pool.wait_ge(s_made, 2)

            def power(src, var, dst, sem_var, sem_out, n):
                pool.sem_inc(s_held, 1)
                nc.gpsimd.tensor_scalar(var, src, 1.0, EPS, ALU.mult, ALU.add).then_inc(sem_var, 1)
                pool.wait_ge(sem_var, n + 1)
                nc.gpsimd.tensor_tensor(dst, var, mhalf[:, 0:dst.shape[1]], ALU.pow).then_inc(sem_out, 1)

            def rstd_of(k, n, t0, T):
                pool.wait_ge(s_mean[k], n + 1)
                power(mv[k][:, t0:t0 + T, 1], lv[k][:, t0:t0 + T], rstd[k][:, t0:t0 + T], s_log[k], s_rstd[k], n)

            with pool.Fori(0, B) as b:
                rstd_of("z", b, 0, NT)
                pool.wait_ge(s_vn, b + 1)
                power(vn[:, :], lv2[:, :], rstd2[:, :], s_log2, s_rstd2, b)
                pool.wait_ge(s_shift, b + 1)
                pool.sem_inc(s_held, 1)
                for t in range(NT):
                    ins = nc.gpsimd.tensor_scalar(zb[:, t, :], x_sb[:, t, :], rstd["z"][:, t:t + 1],
                                                  shift[:, t:t + 1], ALU.mult, ALU.add)
                ins.then_inc(s_zs, 1)
                pool.wait_ge(s_zs, b + 1)
                nc.gpsimd.tensor_tensor(zb[:, :, :], zb[:, :, :],
                                        bproj[:, :].rearrange("p (o d) -> p o d", o=1).to_broadcast([P, NT, D]),
                                        ALU.add).then_inc(s_zb, 1)
                for c in range(2 * KD):
                    pool.wait_ge(s_resid, 2 * KD * b + c + 1)
                    pool.sem_inc(s_held, 1)
                    nc.gpsimd.tensor_scalar(parts[:, c % 2, 1, :], resid[:, :], 1.0, 0.0, ALU.mult, ALU.add)\
                        .then_inc(s_second, 1)
                    pool.wait_ge(s_second, 2 * KD * b + c + 1)
                    nc.gpsimd.tensor_tensor(parts[:, c % 2, 2, :], resid[:, :], parts[:, c % 2, 1, :],
                                            ALU.subtract).then_inc(s_third, 1)
                for k in ("y", "x", "u", "f"):
                    rstd_of(k, b, 0, NT)
            pool.wait_ge(s_x1st, 16 * B)
            pool.wait_ge(s_res, B)
            pool.wait_ge(s_idx, 7)
            for c in range(MT):
                nc.gpsimd.indirect_dma_start(x1[:, c, :], None, x1_dram,
                                             bass.IndirectOffsetOnAxis(ap=idx[:, c:c + 1].bitcast(u32), axis=0))\
                    .then_inc(s_xg, 16)
            rstd_of("x", B, 0, MT)
            rstd_of("u", B, 0, MT)
            rstd_of("u", B + 1, MT, MT)
            rstd_of("f", B, 0, MT)
            pool.wait_ge(s_out, 16 * B)
            pool.wait_ge(s_res, B + 1)
            for c in range(MT):
                nc.gpsimd.indirect_dma_start(out_rows,
                                             bass.IndirectOffsetOnAxis(ap=idx[:, c:c + 1].bitcast(u32), axis=0),
                                             hid[:, c, :], None).then_inc(s_scat, 16)
            pool.wait_ge(s_scat, 16 * MT)

        @block.scalar
        def _(sc):
            def take(base, i):
                sc.wait_ge(s_full, base + i + 1)
                return sbuf2[i % 2]

            def evac_T(base, i, kk, width, scale=1.0, bias=0.0):
                src = take(base, i)
                nc.scalar.activation(zT[:, kk, 0:width], src[:, 0:width], ACT.Identity, scale=scale, bias=bias)\
                    .then_inc(s_free, 1)

            def ffn(base, rbase, i, n, T):
                for kk in range(KD):
                    evac_T(base, i + kk, kk, T * P)
                sc.wait_ge(r_free, rbase + R_FFN + NT // 2)
                nc.scalar.activation(act[:, 0:T, :], hid[:, 0:T, 0:F], ACT.Tanh, scale=0.5).then_inc(s_he, 1)
                evac_T(base, i + KD, 0, T * P, scale=hln[:, 0:1], bias=hln[:, 1:2])

            sc.wait_ge(s_made, 2)
            sc.wait_ge(s_const, C_ALL)
            with sc.Fori(0, B) as b:
                SB = S_BATCH * b
                for kk in range(KD):
                    evac_T(SB, S_ZT + kk, kk, N, scale=lnp[:, 0, kk:kk + 1], bias=lnp[:, 1, kk:kk + 1])
                for c in range(2 * KD):
                    src = take(SB, S_QK + c)
                    if c >= 2:
                        sc.wait_ge(s_resid, 2 * KD * b + c - 1)
                        sc.wait_ge(s_pack[c % 2], 16 * 18 * b + 16 * 6)
                    nc.scalar.activation(qkf[:, c % 2, :], src[:, :], ACT.Copy)
                    nc.scalar.activation(parts[:, c % 2, 0, :], src[:, :], ACT.Copy).then_inc(s_free, 1)
                for e in range(STEPS):
                    for a in range(2):
                        src = take(SB, S_ATT + 2 * e + a)
                        if e >= 2 and a == 0:
                            sc.wait_ge(s_av, STEPS * b + e - 1)
                        nc.scalar.activation(prob[:, e % 2, 2 * a:2 * a + 2, :].rearrange("p g n -> p (g n)"),
                                             src[:, :], ACT.Exp, scale=0.25).then_inc(s_free, 1)
                    if e % 8 == 0 and e > 0:
                        u = e // 8 - 1
                        sc.wait_ge(s_av, STEPS * b + 8 * u + 8)
                        nc.scalar.activation(oT[:, u % 2, :], obank[:, :], ACT.Copy).then_inc(s_oT, 1)
                sc.wait_ge(s_av, STEPS * (b + 1))
                nc.scalar.activation(oT[:, (HU - 1) % 2, :], obank[:, :], ACT.Copy).then_inc(s_oT, 1)
                for kk in range(KD):
                    evac_T(SB, S_AT + kk, kk, N)
                ffn(SB, R_BATCH * b, S_XT, b, NT)
            SB = S_BATCH * B
            for kk in range(KD):
                evac_T(SB, kk, kk, M)
            sc.wait_ge(r_free, R_BATCH * B + 1)
            nc.scalar.activation(gexp[:, :, :], gate[:, :, :], ACT.Tanh, scale=0.5).then_inc(s_ge, 1)
            sc.wait_ge(s_g, 8)
            nc.scalar.activation(ex2[:, :, :], sc2[:, :, :], ACT.Exp).then_inc(s_ge, 1)
            for a in range(E // 2):
                src = take(SB, KD + a)
                nc.scalar.activation(bc[:, 2 * a:2 * a + 2, :].rearrange("p e m -> p (e m)"), src[:, :], ACT.Copy)\
                    .then_inc(s_free, 1)
            sc.wait_ge(r_free, R_BATCH * B + 3)
            nc.scalar.activation(act[:, 0:MT, :], hid[:, 0:MT, 0:F], ACT.Tanh, scale=0.5).then_inc(s_he, 1)
            evac_T(SB, KD + E // 2, 0, M, scale=hln[:, 0:1], bias=hln[:, 1:2])
            sc.wait_ge(r_free, R_BATCH * B + 6)
            nc.scalar.activation(act[:, MT:2 * MT, :], hid[:, MT:2 * MT, 0:F], ACT.Tanh, scale=0.5)\
                .then_inc(s_he, 1)
            evac_T(SB, KD + E // 2 + 1, 1, M, scale=hln[:, 2:3], bias=hln[:, 3:4])

        @block.tensor
        def _(pe):
            def open_s(base, i):
                if i >= 2:
                    pe.wait_ge(s_free, base + i - 1)
                return sbuf2[i % 2]

            def open_r(base, i):
                if i >= 3:
                    pe.wait_ge(r_free, base + i - 2)
                return ring[i % 3]

            def transpose_in(base, i, src, T):
                dst = open_s(base, i)
                for t in range(T):
                    ins = nc.tensor.transpose(dst[:, t * P:(t + 1) * P], src[:, t, :], ident[:, :])
                ins.then_inc(s_full, 1)

            def project(base, i, t0, T, w, kd):
                dst = open_r(base, i)
                for t in range(t0, t0 + 2):
                    for k in range(kd):
                        ins = nc.tensor.matmul(dst[:, (t - t0) * D:(t - t0 + 1) * D], zT[:, k, t * P:(t + 1) * P],
                                               w[:, k, :], start=(k == 0), stop=(k == kd - 1))
                ins.then_inc(r_full, 1)

            pe.wait_ge(s_made, 1)
            pe.wait_ge(s_const, C_ALL)
            pe.wait_ge(s_vset, 1)
            w3k = w3[:, :].rearrange("p (o d) -> p o d", o=1)
            with pe.Fori(0, B) as b:
                SB, RB = S_BATCH * b, R_BATCH * b
                pe.wait_ge(s_norm["z"], b + 1)
                for kk in range(KD):
                    transpose_in(SB, S_ZT + kk, zn[:, :, kk * P:(kk + 1) * P], NT)
                pe.wait_ge(s_free, SB + S_ZT + KD)
                for c in range(2 * KD):
                    w = wk if c < KD else wq
                    dst = open_s(SB, S_QK + c)
                    for h in range(NH):
                        for k in range(KD):
                            ins = nc.tensor.matmul(dst[:, h * HALF:(h + 1) * HALF],
                                                   w[:, k, (c % KD) * P:(c % KD + 1) * P],
                                                   zT[:, k, h * HALF:(h + 1) * HALF],
                                                   start=(k == 0), stop=(k == KD - 1))
                    ins.then_inc(s_full, 1)
                for i in range(NT // 2):
                    project(RB, R_V + i, 2 * i, NT, wv, KD)
                pe.wait_ge(s_made, 2)
                pe.wait_ge(s_pack[0], 16 * 18 * (b + 1))
                pe.wait_ge(s_pack[1], 16 * 18 * (b + 1))
                pe.wait_ge(r_free, RB + R_ATT)
                r = R_ATT
                for slot in range(SLOTS):
                    e = slot - LEAD

                    def max_products(js):
                        nonlocal r
                        u = slot // 8
                        g, qh = u // NH, u % NH
                        for j in js:
                            n = (slot % 8) * 4 + j
                            h, qt, kh = g * GH + n // (2 * QT), (n // 2) % QT, n % 2
                            dst = open_r(RB, r)
                            nc.tensor.matmul(dst[:, :], qp[0:KR, qh, h, qt * P:(qt + 1) * P],
                                             kp[0:KR, h, kh * HALF:(kh + 1) * HALF],
                                             start=True, stop=True).then_inc(r_full, 1)
                            r += 1

                    def scores(a):
                        u, kt = e // 8, e % 8
                        g, qh = u // NH, u % NH
                        dst = open_s(SB, S_ATT + 2 * e + a)
                        if kt == 0 and a == 0:
                            pe.wait_ge(s_mrow[u % 2], 32 * (HU // 2 * b + u // 2 + 1))
                        for j in range(2):
                            h = g * GH + 2 * a + j
                            ins = nc.tensor.matmul(dst[:, j * HALF:(j + 1) * HALF],
                                                   kp[0:KM, h, kt * P:(kt + 1) * P], qp[0:KM, qh, h, :],
                                                   start=True, stop=True)
                        ins.then_inc(s_full, 1)

                    def value_product(v):
                        u, kt = v // 8, v % 8
                        g = u // NH
                        if kt == 0 and u > 0:
                            pe.wait_ge(s_oT, HU * b + u)
                        pe.wait_ge(s_free, SB + S_ATT + 2 * v + 2)
                        for i in range(GH):
                            ins = nc.tensor.matmul(obank[i * VW:(i + 1) * VW, :], vaug[:, kt, g * GH + i, :],
                                                   prob[:, v % 2, i, :], start=(kt == 0), stop=(kt == NT - 1))
                        ins.then_inc(s_av, 1)

                    if 0 <= e < STEPS:
                        scores(0)
                    if slot < STEPS:
                        max_products(range(0, 2))
                    if 0 <= e < STEPS:
                        scores(1)
                    if 0 <= e - 1 < STEPS:
                        value_product(e - 1)
                    if slot < STEPS:
                        max_products(range(2, 4))
                    if slot % 8 == 1 and 0 <= slot // 8 - 1 < HU:
                        u = slot // 8 - 1
                        dst = open_r(RB, r)
                        pe.wait_ge(s_nm, HU * b + u + 1)
                        nc.tensor.transpose(dst[0:GH * QT, 0:P], nm[:, u % 2, :], ident[:, :]).then_inc(r_full, 1)
                        r += 1
                    if e >= 0 and e % 8 == 2 and 0 <= e // 8 - 1 < HU:
                        u = e // 8 - 1
                        dst = open_r(RB, r)
                        pe.wait_ge(s_oT, HU * b + u + 1)
                        for c in range(QT):
                            ins = nc.tensor.transpose(dst[:, c * P:(c + 1) * P], oT[:, u % 2, c * P:(c + 1) * P],
                                                      ident[:, :])
                        ins.then_inc(r_full, 1)
                        r += 1
                assert r == R_PROJ
                pe.wait_ge(r_free, RB + R_PROJ)
                for kk in range(KD):
                    transpose_in(SB, S_AT + kk, anat[:, :, kk * P:(kk + 1) * P], NT)
                pe.wait_ge(s_free, SB + S_AT + KD)
                for i in range(NT // 2):
                    project(RB, R_PROJ + i, 2 * i, NT, wp, KD)
                pe.wait_ge(s_norm["x"], b + 1)
                for kk in range(KD):
                    transpose_in(SB, S_XT + kk, zn[:, :, kk * P:(kk + 1) * P], NT)
                pe.wait_ge(s_free, SB + S_XT + KD)
                for i in range(NT // 2):
                    project(RB, R_FFN + i, 2 * i, NT, w12, KD)
                pe.wait_ge(s_norm["u"], b + 1)
                transpose_in(SB, S_UT, act, NT)
                pe.wait_ge(s_free, SB + S_UT + 1)
                for i in range(NT // 2):
                    project(RB, R_FFN + NT // 2 + i, 2 * i, NT, w3k, 1)
            SB, RB = S_BATCH * B, R_BATCH * B
            pe.wait_ge(s_norm["x"], B + 1)
            for kk in range(KD):
                transpose_in(SB, kk, zn[:, :, kk * P:(kk + 1) * P], MT)
            pe.wait_ge(s_free, SB + KD)
            dst = open_r(RB, 0)
            for c in range(MT):
                for k in range(KD):
                    ins = nc.tensor.matmul(dst[:, c * 16:c * 16 + 1 + E], zT[:, k, c * P:(c + 1) * P], wg[:, k, :],
                                           start=(k == 0), stop=(k == KD - 1))
            ins.then_inc(r_full, 1)
            for i in range(MT // 2):
                project(RB, 1 + i, 2 * i, MT, w12, KD)
            pe.wait_ge(s_g, 6)
            dst = open_r(RB, 3)
            for c in range(MT):
                ins = nc.tensor.transpose(dst[0:E, c * P:(c + 1) * P], onehot[:, c, :], ident[:, :])
            ins.then_inc(r_full, 1)
            pe.wait_ge(r_free, RB + 4)
            for a in range(E // 2):
                dst = open_s(SB, KD + a)
                for j in range(2):
                    ins = nc.tensor.matmul(dst[:, j * M:(j + 1) * M], pick[:, 2 * a + j, :], ohT,
                                           start=True, stop=True)
                ins.then_inc(s_full, 1)
            pe.wait_ge(s_norm["u"], B + 1)
            transpose_in(SB, KD + E // 2, act, MT)
            pe.wait_ge(s_we, 32)
            pe.wait_ge(s_xm, 1)
            for i in range(MT // 2):
                dst = open_r(RB, 4 + i)
                for t in range(2):
                    m = slice((2 * i + t) * P, (2 * i + t + 1) * P)
                    o = dst[:, t * D:(t + 1) * D]
                    nc.tensor.matmul(o, qkf[0:E, 0, m], eb12[:, :], start=True, stop=False)
                    for k in range(KD):
                        for e in range(E):
                            ins = nc.tensor.matmul(o, xm[:, k, e, m], we12[:, k, e, :], start=False,
                                                   stop=(k == KD - 1 and e == E - 1))
                ins.then_inc(r_full, 1)
            pe.wait_ge(s_free, SB + KD + E // 2 + 1)
            for i in range(MT // 2):
                project(RB, 6 + i, 2 * i, MT, w3k, 1)
            pe.wait_ge(s_norm["u"], B + 2)
            transpose_in(SB, KD + E // 2 + 1, act[:, MT:2 * MT, :], MT)
            pe.wait_ge(s_xm, 2)
            for i in range(MT // 2):
                dst = open_r(RB, 8 + i)
                for t in range(2):
                    m = slice((2 * i + t) * P, (2 * i + t + 1) * P)
                    o = dst[:, t * D:(t + 1) * D]
                    nc.tensor.matmul(o, qkf[0:E, 0, m], ebo[:, :], start=True, stop=False)
                    for e in range(E):
                        ins = nc.tensor.matmul(o, zm[:, e, m], we3[:, e, :], start=False, stop=(e == E - 1))
                ins.then_inc(r_full, 1)

        @block.vector
        def _(ve):
            def take(base, i):
                ve.wait_ge(r_full, base + i + 1)
                return ring[i % 3]

            def stats(k, src, n, t0, T, width):
                for t in range(t0, t0 + T):
                    ins = nc.vector.bn_stats(st6[:, t, :], src[:, t, 0:width])
                ins.then_inc(s_stats[k], 1)
                ve.wait_ge(s_stats[k], n + 1)
                ve.sem_inc(s_held, 1)
                for t in range(t0, t0 + T):
                    ins = nc.vector.bn_aggr(mv[k][:, t, :], st6[:, t, :])
                ins.then_inc(s_mean[k], 1)

            def normalize(k, dst, src, scale, t0, T, width):
                for t in range(t0, t0 + T):
                    ins = nc.vector.tensor_scalar(dst[:, t, 0:width], src[:, t, 0:width], mv[k][:, t, 0:1],
                                                  scale[:, t:t + 1], ALU.subtract, ALU.mult)
                ins.then_inc(s_norm[k], 1)

            def add_bias(base, i, t, dst, bias):
                src = take(base, i)
                return nc.vector.tensor_tensor(dst[:, t:t + 2, :], src[:, :].rearrange("p (t d) -> p t d", t=2),
                                               bias[:, :].rearrange("p (o d) -> p o d", o=1)
                                               .to_broadcast([P, 2, D]), ALU.add).then_inc(r_free, 1)

            def gated(n, h, t0, T):
                a = act[:, t0:t0 + T, :]
                nc.vector.scalar_tensor_tensor(a, a, 1.0, h[:, t0:t0 + T, 0:F], ALU.add, ALU.mult)\
                    .then_inc(s_hc, 1)
                ve.wait_ge(s_hc, 2 * n + 1)
                nc.vector.scalar_tensor_tensor(a, a, 0.5, h[:, t0:t0 + T, F:2 * F], ALU.mult, ALU.mult)\
                    .then_inc(s_hc, 1)
                ve.wait_ge(s_hc, 2 * n + 2)

            def finish(n, T):
                stats("f", hid, n, 0, T, D)
                ve.wait_ge(s_rstd["f"], n + 1)
                normalize("f", hid, hid, rstd["f"], 0, T, D)
                ve.wait_ge(s_norm["f"], n + 1)
                nc.vector.tensor_tensor(hid[:, 0:T, :], hid[:, 0:T, :], x1[:, 0:T, :], ALU.add)\
                    .then_inc(s_res, 1)

            nc.vector.memset(vaug[:, :, :, :], 0.0).then_inc(s_small, 1)
            ve.wait_ge(s_small, 1)
            nc.vector.memset(vaug[:, :, :, HD:HD + 1], 1.0).then_inc(s_vset, 1)
            ve.wait_ge(s_idxin, 32)
            nc.vector.tensor_copy(idxf[:, :, :], idx_in[:, :, :]).then_inc(s_idx, 1)
            ve.wait_ge(s_idx, 1)
            nc.vector.tensor_scalar(idxn[:, 0, :], idxf[:, 0, :], 0.0, float(B), ALU.is_lt, ALU.mult)
            nc.vector.tensor_scalar(idxn[:, 1, :], idxf[:, 1, :], 0.0, float(N), ALU.is_lt, ALU.mult)\
                .then_inc(s_idx, 1)
            ve.wait_ge(s_idx, 2)
            nc.vector.tensor_tensor(idxf[:, :, :], idxf[:, :, :], idxn[:, :, :], ALU.add).then_inc(s_idx, 1)
            ve.wait_ge(s_idx, 3)
            nc.vector.tensor_scalar(idxn[:, 0, :], idxf[:, 0, :], float(N), None, ALU.mult).then_inc(s_idx, 1)
            ve.wait_ge(s_idx, 4)
            nc.vector.tensor_tensor(idxn[:, 1, :], idxn[:, 0, :], idxf[:, 1, :], ALU.add).then_inc(s_idx, 1)
            ve.wait_ge(s_idx, 5)
            nc.vector.tensor_copy(idx[:, :], idxn[:, 1, :]).then_inc(s_idx, 1)
            ve.wait_ge(s_iota, 1)
            nc.vector.tensor_copy(iota[:, :], iotai[:, :]).then_inc(s_idx, 1)
            ve.wait_ge(s_const, C_ALL)

            with ve.Fori(0, B) as b:
                RB = R_BATCH * b
                ve.wait_ge(s_xin, 16 * (b + 1))
                stats("z", x_sb, b, 0, NT, D)
                ve.wait_ge(s_rstd["z"], b + 1)
                nc.vector.tensor_tensor(rr[:, :], rstd["z"][:, :], rstd["z"][:, :], ALU.mult).then_inc(s_small, 1)
                nc.vector.scalar_tensor_tensor(shift[:, :], mv["z"][:, :, 0], -1.0, rstd["z"][:, :],
                                               ALU.mult, ALU.mult).then_inc(s_shift, 1)
                ve.wait_ge(s_small, 2 * b + 2)
                nc.vector.tensor_tensor(vn[:, :], rr[:, :], mv["z"][:, :, 1], ALU.mult).then_inc(s_vn, 1)
                ve.wait_ge(s_rstd2, b + 1)
                nc.vector.tensor_tensor(r12[:, :], rstd["z"][:, :], rstd2[:, :], ALU.mult).then_inc(s_small, 1)
                ve.wait_ge(s_small, 2 * b + 3)
                normalize("z", zn, x_sb, r12, 0, NT, D)
                for c in range(2 * KD):
                    ve.wait_ge(s_free, S_BATCH * b + S_QK + c + 1)
                    if c >= 1:
                        ve.wait_ge(s_third, 2 * KD * b + c)
                    nc.vector.tensor_tensor(resid[:, :], qkf[:, c % 2, :], parts[:, c % 2, 0, :],
                                            ALU.subtract).then_inc(s_resid, 1)
                for i in range(NT // 2):
                    src = take(RB, R_V + i)
                    ins = nc.vector.tensor_copy(vaug[:, 2 * i:2 * i + 2, :, 0:HD],
                                                src[:, :].rearrange("p (t h d) -> p t h d", t=2, h=H))
                    ins.then_inc(r_free, 1)
                for i, item in enumerate(ATT):
                    src = take(RB, R_ATT + i)
                    if item[0] == "max":
                        _, slot, j = item
                        u, n = slot // 8, (slot % 8) * 4 + j
                        nc.vector.tensor_reduce(mx[:, u % 2, n:n + 1], src[:, :], AX.X, ALU.max)\
                            .then_inc(r_free, 1)
                        if n == 4 * 8 - 1:
                            ve.wait_ge(r_free, RB + R_ATT + i + 1)
                            nc.vector.tensor_reduce(nm[:, u % 2, :],
                                                    mx[:, u % 2, :].rearrange("p (n k) -> p n k", k=2),
                                                    AX.X, ALU.max, negate=True).then_inc(s_nm, 1)
                    elif item[0] == "mt":
                        u = item[1]
                        nc.vector.tensor_copy(mp[:, u % 2, 0, :], src[0:GH * QT, 0:P]).then_inc(s_m1, 1)
                        ve.wait_ge(s_m1, HU * b + u + 1)
                        nc.vector.tensor_tensor(mp[:, u % 2, 1, :], src[0:GH * QT, 0:P], mp[:, u % 2, 0, :],
                                                ALU.subtract).then_inc(r_free, 1)
                    else:
                        u = item[1]
                        g, qh = u // NH, u % NH
                        o = src[:, :].rearrange("p (c n) -> p c n", n=VW)
                        ve.wait_ge(r_free, RB + R_ATT + i)
                        nc.vector.reciprocal(rsum[:, :], o[:, :, HD]).then_inc(s_rs, 1)
                        ve.wait_ge(s_rs, HU * b + u + 1)
                        o4 = src[:, :].rearrange("p (q h n) -> p q h n", h=GH, n=VW)
                        r4 = rsum[:, :].rearrange("p (q h o) -> p q h o", h=GH, o=1)\
                            .to_broadcast([P, QT, GH, HD])
                        a4 = anat[:, qh * QT:(qh + 1) * QT, g * GH * HD:(g + 1) * GH * HD]\
                            .rearrange("p q (h d) -> p q h d", h=GH)
                        nc.vector.tensor_tensor(a4, o4[:, :, :, 0:HD], r4, ALU.mult).then_inc(r_free, 1)
                ve.wait_ge(s_zb, b + 1)
                for i in range(NT // 2):
                    src = take(RB, R_PROJ + i)
                    nc.vector.tensor_tensor(x1[:, 2 * i:2 * i + 2, :], src[:, :].rearrange("p (t d) -> p t d", t=2),
                                            zb[:, 2 * i:2 * i + 2, :], ALU.add).then_inc(r_free, 1)
                ve.wait_ge(r_free, RB + R_PROJ + NT // 2)
                stats("y", x1, b, 0, NT, D)
                ve.wait_ge(s_rstd["y"], b + 1)
                normalize("y", x1, x1, rstd["y"], 0, NT, D)
                ve.wait_ge(s_norm["y"], b + 1)
                nc.vector.tensor_tensor(x1[:, :, :], x1[:, :, :], x_sb[:, :, :], ALU.add).then_inc(s_x1, 1)
                ve.wait_ge(s_x1, b + 1)
                stats("x", x1, b, 0, NT, D)
                ve.wait_ge(s_rstd["x"], b + 1)
                normalize("x", zn, x1, rstd["x"], 0, NT, D)
                for i in range(NT // 2):
                    add_bias(RB, R_FFN + i, 2 * i, hid, b12)
                ve.wait_ge(s_he, b + 1)
                gated(b, hid, 0, NT)
                stats("u", act, b, 0, NT, F)
                ve.wait_ge(s_rstd["u"], b + 1)
                normalize("u", act, act, rstd["u"], 0, NT, F)
                for i in range(NT // 2):
                    add_bias(RB, R_FFN + NT // 2 + i, 2 * i, hid, b3)
                ve.wait_ge(r_free, RB + R_BATCH)
                finish(b, NT)

            RB = R_BATCH * B
            ve.wait_ge(s_xg, 16 * MT)
            stats("x", x1, B, 0, MT, D)
            ve.wait_ge(s_rstd["x"], B + 1)
            normalize("x", zn, x1, rstd["x"], 0, MT, D)
            src = take(RB, 0)
            nc.vector.tensor_tensor(gate[:, :, :], src[:, 0:16 * MT].rearrange("p (c n) -> p c n", n=16)[:, :, 0:1 + E],
                                    bgate[:, :].rearrange("p (o n) -> p o n", o=1).to_broadcast([P, MT, 1 + E]),
                                    ALU.add).then_inc(r_free, 1)
            ve.wait_ge(s_out, 16 * B)
            for i in range(MT // 2):
                add_bias(RB, 1 + i, 2 * i, hid, b12)
            ve.wait_ge(s_ge, 1)
            nc.vector.tensor_scalar(gate[:, :, :], gexp[:, :, :], 0.5, 0.5, ALU.mult, ALU.add).then_inc(s_g, 2)
            ve.wait_ge(s_g, 2)
            nc.vector.tensor_tensor(gsel[:, :, :], gate[:, :, 1:1 + E],
                                    bexp[:, :].rearrange("p (o n) -> p o n", o=1).to_broadcast([P, MT, E]),
                                    ALU.add).then_inc(s_g, 1)
            ve.wait_ge(s_g, 3)
            for c in range(MT):
                ins = nc.vector.max(top8[:, c, :], gsel[:, c, :])
            ins.then_inc(s_g, 1)
            ve.wait_ge(s_g, 4)
            for c in range(MT):
                ins = nc.vector.max_index(topi[:, c, :], top8[:, c, :], gsel[:, c, :])
            ins.then_inc(s_mix, 1)
            ve.wait_ge(s_mix, 1)
            nc.vector.tensor_copy(topf[:, :], topi[:, :, 0]).then_inc(s_g, 1)
            ve.wait_ge(s_g, 5)
            for c in range(MT):
                ins = nc.vector.tensor_scalar(onehot[:, c, :], iota[:, :], topf[:, c:c + 1], None, ALU.is_equal)
            ins.then_inc(s_g, 1)
            ve.wait_ge(s_g, 6)
            nc.vector.tensor_tensor(ohs[:, :, :], onehot[:, :, :], gate[:, :, 1:1 + E], ALU.mult).then_inc(s_g, 1)
            ve.wait_ge(s_g, 7)
            nc.vector.tensor_copy(sc2[:, :, 0], gate[:, :, 0])
            nc.vector.tensor_reduce(sc2[:, :, 1], ohs[:, :, :], AX.X, ALU.add).then_inc(s_g, 1)
            src = take(RB, 3)
            nc.vector.tensor_copy(ohT, src[0:E, 0:M]).then_inc(r_free, 1)
            ve.wait_ge(s_ge, 2)
            nc.vector.tensor_reduce(sum2[:, :], ex2[:, :, :], AX.X, ALU.add).then_inc(s_mix, 1)
            ve.wait_ge(s_mix, 2)
            nc.vector.reciprocal(sum2[:, :], sum2[:, :]).then_inc(s_mix, 1)
            ve.wait_ge(s_mix, 3)
            nc.vector.tensor_tensor(wt2[:, :, :], ex2[:, :, :],
                                    sum2[:, :].rearrange("p (c o) -> p c o", o=1).to_broadcast([P, MT, 2]),
                                    ALU.mult).then_inc(s_mix, 1)
            ve.wait_ge(s_free, S_BATCH * B + KD + E // 2)
            for k in range(KD):
                for e in range(E):
                    ins = nc.vector.tensor_tensor(xm[:, k, e, :], zT[:, k, 0:M], bc[:, e, :], ALU.mult)
            ins.then_inc(s_xm, 1)
            ve.wait_ge(s_he, B + 1)
            gated(B, hid, 0, MT)
            stats("u", act, B, 0, MT, F)
            ve.wait_ge(s_rstd["u"], B + 1)
            normalize("u", act, act, rstd["u"], 0, MT, F)
            for i in range(MT // 2):
                src = take(RB, 4 + i)
                nc.vector.tensor_copy(hid[:, MT + 2 * i:MT + 2 * i + 2, :],
                                      src[:, :].rearrange("p (t d) -> p t d", t=2)).then_inc(r_free, 1)
            for i in range(MT // 2):
                add_bias(RB, 6 + i, 2 * i, hid, b3)
            ve.wait_ge(s_he, B + 2)
            gated(B + 1, hid, MT, MT)
            stats("u", act, B + 1, MT, MT, F)
            ve.wait_ge(s_rstd["u"], B + 2)
            normalize("u", act, act, rstd["u"], MT, MT, F)
            ve.wait_ge(s_free, S_BATCH * B + KD + E // 2 + 2)
            for e in range(E):
                ins = nc.vector.tensor_tensor(zm[:, e, :], zT[:, 1, 0:M], bc[:, e, :], ALU.mult)
            ins.then_inc(s_xm, 1)
            for c in range(MT):
                src = take(RB, 8 + c // 2)
                ve.wait_ge(s_mix, 4 + 2 * c)
                ins = nc.vector.tensor_scalar(mout, src[:, (c % 2) * D:(c % 2 + 1) * D], wt2[:, c, 1:2], None,
                                              ALU.mult).then_inc(s_mix, 1)
                ve.wait_ge(s_mix, 5 + 2 * c)
                nc.vector.scalar_tensor_tensor(hid[:, c, :], hid[:, c, :], wt2[:, c, 0:1], mout,
                                               ALU.mult, ALU.add).then_inc(s_mix, 1)
            ve.wait_ge(s_mix, 4 + 2 * MT)
            finish(B, MT)


def kernel(L0_attn_z, L0_attn_ln_scale, L0_attn_ln_bias, L0_attn_w_qkv, L0_attn_w_proj, L0_attn_b_proj,
           L0_ffn_index_b, L0_ffn_index_t, L0_ffn_sw1, L0_ffn_sb1, L0_ffn_sw2, L0_ffn_sb2, L0_ffn_sw3, L0_ffn_sb3,
           L0_ffn_s_ln_g, L0_ffn_s_ln_b, L0_ffn_sg_w, L0_ffn_sg_b, L0_ffn_eg_w, L0_ffn_eg_b, L0_ffn_exp_bias,
           L0_ffn_ew1, L0_ffn_eb1, L0_ffn_ew2, L0_ffn_eb2, L0_ffn_ew3, L0_ffn_eb3, L0_ffn_sel_ln_g,
           L0_ffn_sel_ln_b):
    import numpy as np
    import concourse.bacc as bacc
    from concourse.bass_utils import run_bass_kernel_spmd

    w_qkv = np.asarray(L0_attn_w_qkv).reshape(D, H, HD, 3)

    def tiles_of_8_heads(w):
        return w.reshape(D, 2, 8, HD).transpose(0, 1, 3, 2).reshape(D, D)

    sw1, sw2, ew1, ew2, ew3 = (np.asarray(a) for a in (L0_ffn_sw1, L0_ffn_sw2, L0_ffn_ew1, L0_ffn_ew2, L0_ffn_ew3))
    ln_params = np.stack([np.asarray(L0_attn_ln_scale), np.asarray(L0_attn_ln_bias)]).reshape(2, KD, P)
    arrays = {
        "x": L0_attn_z, "ln_params": ln_params.transpose(2, 0, 1),
        "w_q": tiles_of_8_heads(w_qkv[..., 0]), "w_k": tiles_of_8_heads(w_qkv[..., 1]),
        "w_v": w_qkv[..., 2].reshape(D, D), "w_proj": L0_attn_w_proj, "b_proj": L0_attn_b_proj,
        "index_b": L0_ffn_index_b, "index_t": L0_ffn_index_t,
        "sw12": np.concatenate([sw1.T, sw2.T], axis=1),
        "sb12": np.concatenate([np.asarray(L0_ffn_sb1), np.asarray(L0_ffn_sb2)]),
        "sw3": np.asarray(L0_ffn_sw3).T, "sb3": L0_ffn_sb3,
        "hidden_ln": np.stack([np.asarray(a) for a in (L0_ffn_s_ln_g, L0_ffn_s_ln_b, L0_ffn_sel_ln_g,
                                                       L0_ffn_sel_ln_b)], axis=1),
        "gate_w": np.concatenate([np.asarray(L0_ffn_sg_w).T, np.asarray(L0_ffn_eg_w).T], axis=1),
        "gate_b": np.concatenate([np.asarray(L0_ffn_sg_b), np.asarray(L0_ffn_eg_b)]),
        "exp_bias": L0_ffn_exp_bias,
        "ew12": np.concatenate([ew1.transpose(2, 0, 1), ew2.transpose(2, 0, 1)], axis=2),
        "ebias12": np.concatenate([np.asarray(L0_ffn_eb1), np.asarray(L0_ffn_eb2)], axis=1),
        "ew3": ew3.transpose(2, 0, 1), "eb3": L0_ffn_eb3,
    }
    arrays = {k: np.ascontiguousarray(v) for k, v in arrays.items()}
    nc = bacc.Bacc("TRN2", target_bir_lowering=False, num_devices=1)
    args = [nc.dram_tensor(k, a.shape, mybir.dt.from_np(a.dtype), kind="ExternalInput").ap()
            for k, a in arrays.items()]
    args.append(nc.dram_tensor("out", (B, N, D), mybir.dt.float32, kind="ExternalOutput").ap())
    build(nc, *args)
    r = run_bass_kernel_spmd(nc, [arrays], core_ids=[0])
    return r.results[0]["out"]
```
